# Optimizing a Trainium2 kernel written in Bass

```python
import numpy as np
import jax
import jax.numpy as jnp

def _softmax(x, axis=-1):
    return jax.nn.softmax(x, axis=axis)

def _gelu(x):
    return jax.nn.gelu(x, approximate=True)

def _silu(x):
    return jax.nn.silu(x)

def _sigmoid(x):
    return jax.nn.sigmoid(x)

def _layernorm(x, axis=-1, eps=1e-05):
    m = jnp.mean(x, axis=axis, keepdims=True)
    v = jnp.var(x, axis=axis, keepdims=True)
    return (x - m) / jnp.sqrt(v + eps)

def _scatter_add(tgt, idx, src, axis=0):
    return tgt.at[idx].add(src)

def _segment_sum(src, seg, n):
    return jax.ops.segment_sum(src, seg, n)
kernel_name = 'mk_gnn_resnorm_d4_gnn_r16_d9d83b'

def setup_inputs(seed: int=0):
    np.random.seed(seed)
    _w = jnp.asarray

    def _rec_inputs():
        import jax
        import jax.numpy as jnp
        _gk = jax.random.key(seed)
        x = -0.000202 + 1 * jax.random.normal(jax.random.fold_in(_gk, 1), (3125, 256), jnp.float32)
        _s = jax.random.randint(jax.random.fold_in(_gk, 2), (25000,), 0, 3125, jnp.int32)
        _d = jax.random.randint(jax.random.fold_in(_gk, 3), (25000,), 0, 3125, jnp.int32)
        _loop = jnp.arange(3125, dtype=jnp.int32)
        src = jnp.concatenate([_s, _d, _loop])
        dst = jnp.concatenate([_d, _s, _loop])
        _o = jnp.argsort(dst, stable=True)
        src = src[_o]
        dst = dst[_o]
        edge_attr_64 = -5.3897e-05 + 0.999841 * jax.random.normal(jax.random.fold_in(_gk, 12), (53125, 64), jnp.float32)
        edge_type_8 = jax.random.randint(jax.random.fold_in(_gk, 14), (53125,), 0, 8, jnp.int32)
        edge_weight1 = jax.random.uniform(jax.random.fold_in(_gk, 15), (53125, 1), jnp.float32, 0.0, 0.999998)
        return (x, src, dst, edge_attr_64, edge_type_8, edge_weight1)
    x, src, dst, edge_attr_64, edge_type_8, edge_weight1 = _rec_inputs()

    def _L0_gnn_setup():
        import jax, jax.numpy as jnp
        import numpy as np
        LOG2 = float(np.log(2.0))

        def ssp(x):
            return jax.nn.softplus(x) - LOG2
        N_ATOMS, N_EDGES, N_HF, N_RBF = (25000, 25000, 256, 64)
        key = jax.random.key(seed)
        ks = jax.random.split(key, 16)
        s = 1.0 / np.sqrt(N_HF)
        sr = 1.0 / np.sqrt(N_RBF)
        return {'x': jax.random.normal(ks[0], (N_ATOMS, N_HF), jnp.float32), 'rbf': jax.random.normal(ks[1], (N_EDGES, N_RBF), jnp.float32), 'dist_cut': jax.random.uniform(ks[2], (N_EDGES, 1), jnp.float32), 'idx_i': jax.random.randint(ks[3], (N_EDGES,), 0, N_ATOMS), 'idx_j': jax.random.randint(ks[4], (N_EDGES,), 0, N_ATOMS), 'W_in2f': jax.random.normal(ks[5], (N_HF, N_HF), jnp.float32) * s, 'Wf1': jax.random.normal(ks[6], (N_RBF, N_HF), jnp.float32) * sr, 'bf1': jnp.zeros((N_HF,), jnp.float32), 'Wf2': jax.random.normal(ks[7], (N_HF, N_HF), jnp.float32) * s, 'bf2': jnp.zeros((N_HF,), jnp.float32), 'Wo1': jax.random.normal(ks[8], (N_HF, N_HF), jnp.float32) * s, 'bo1': jnp.zeros((N_HF,), jnp.float32), 'Wo2': jax.random.normal(ks[9], (N_HF, N_HF), jnp.float32) * s, 'bo2': jnp.zeros((N_HF,), jnp.float32)}
    _L0_gnn_all = _L0_gnn_setup()
    _L0_gnn_in = {k: v for k, v in _L0_gnn_all.items() if k in ('W_in2f', 'Wf1', 'bf1', 'Wf2', 'bf2', 'Wo1', 'bo1', 'Wo2', 'bo2')}
    del _L0_gnn_all

    def _L1_gnn_setup():
        import jax, jax.numpy as jnp
        import numpy as np
        DIM = 256
        H = 8
        HD = DIM // H
        N = 3125
        E = 50000
        FFN = 4 * DIM
        EPS = 1e-05

        def layer_norm(x, g, b):
            mu = jnp.mean(x, axis=-1, keepdims=True)
            var = jnp.mean((x - mu) ** 2, axis=-1, keepdims=True)
            return (x - mu) * jax.lax.rsqrt(var + EPS) * g + b

        def _mhsa(h, edge_bias, src, dst, Wq, Wk, Wv, Wp, bp):
            n = h.shape[0]
            Q = (h @ Wq).reshape(n, H, HD)
            K = (h @ Wk).reshape(n, H, HD)
            V = (h @ Wv).reshape(n, H, HD)
            score = jnp.einsum('ehd,ehd->eh', K[src], Q[dst]) / np.sqrt(HD) + edge_bias
            m = jax.ops.segment_max(score, dst, num_segments=n)
            ex = jnp.exp(score - m[dst])
            denom = jax.ops.segment_sum(ex, dst, num_segments=n)
            attn = ex / denom[dst]
            out = jax.ops.segment_sum(attn[:, :, None] * V[src], dst, num_segments=n)
            return out.reshape(n, DIM) @ Wp + bp
        key = jax.random.key(seed)
        ks = jax.random.split(key, 16)
        s = 1.0 / np.sqrt(DIM)
        inp = {'h': jax.random.normal(ks[0], (N, DIM), jnp.float32), 'edge_bias': jax.random.normal(ks[1], (E, 1), jnp.float32), 'src': jax.random.randint(ks[2], (E,), 0, N, jnp.int32), 'dst': jax.random.randint(ks[3], (E,), 0, N, jnp.int32), 'Wq': jax.random.normal(ks[4], (DIM, DIM), jnp.float32) * s, 'Wk': jax.random.normal(ks[5], (DIM, DIM), jnp.float32) * s, 'Wv': jax.random.normal(ks[6], (DIM, DIM), jnp.float32) * s, 'Wp': jax.random.normal(ks[7], (DIM, DIM), jnp.float32) * s, 'bp': jnp.zeros((DIM,), jnp.float32), 'ln1_g': jnp.ones((DIM,), jnp.float32), 'ln1_b': jnp.zeros((DIM,), jnp.float32), 'ln2_g': jnp.ones((DIM,), jnp.float32), 'ln2_b': jnp.zeros((DIM,), jnp.float32), 'W1': jax.random.normal(ks[8], (DIM, FFN), jnp.float32) * s, 'b1': jnp.zeros((FFN,), jnp.float32), 'W2': jax.random.normal(ks[9], (FFN, DIM), jnp.float32) * (1.0 / np.sqrt(FFN)), 'b2': jnp.zeros((DIM,), jnp.float32)}
        return inp
    _L1_gnn_all = _L1_gnn_setup()
    _L1_gnn_in = {k: v for k, v in _L1_gnn_all.items() if k in ('Wq', 'Wk', 'Wv', 'Wp', 'bp', 'ln1_g', 'ln1_b', 'ln2_g', 'ln2_b', 'W1', 'b1', 'W2', 'b2')}
    del _L1_gnn_all

    def _L2_gnn_setup():
        import jax, jax.numpy as jnp
        import numpy as np
        N_NODES = 3125
        N_EDGES = 50000
        IN_CH = 256
        HID_CH = 256
        OUT_CH = 256
        N_LAYERS = 3
        key = jax.random.key(seed)
        ks = jax.random.split(key, 8)
        s_in = 1.0 / np.sqrt(IN_CH)
        s_h = 1.0 / np.sqrt(HID_CH)
        return {'x': jax.random.normal(ks[0], (N_NODES, IN_CH), dtype=jnp.float32), 'W_in': jax.random.normal(ks[1], (IN_CH, HID_CH), dtype=jnp.float32) * s_in, 'b_in': jnp.zeros((HID_CH,), dtype=jnp.float32), 'W_agg': jax.random.normal(ks[2], (N_LAYERS, HID_CH, HID_CH), dtype=jnp.float32) * s_h, 'W_self': jax.random.normal(ks[3], (N_LAYERS, HID_CH, HID_CH), dtype=jnp.float32) * s_h, 'b_hid': jnp.zeros((N_LAYERS, HID_CH), dtype=jnp.float32), 'W_out': jax.random.normal(ks[4], (HID_CH, OUT_CH), dtype=jnp.float32) * s_h, 'b_out': jnp.zeros((OUT_CH,), dtype=jnp.float32), 'edge_index': jax.random.randint(ks[5], (2, N_EDGES), 0, N_NODES, dtype=jnp.int64)}
    _L2_gnn_all = _L2_gnn_setup()
    _L2_gnn_in = {k: v for k, v in _L2_gnn_all.items() if k in ('W_in', 'b_in', 'W_agg', 'W_self', 'b_hid', 'W_out', 'b_out')}
    del _L2_gnn_all

    def _L3_gnn_setup():
        import jax, jax.numpy as jnp
        import numpy as np
        N = 3125
        E = 50000
        DIN = 256
        DH = 256
        DOUT = 256
        R = 8
        B = 4

        def rgcn_conv(x, src, dst, edge_type, basis, comp, root, bias):
            xb = jnp.einsum('ni,bio->nbo', x, basis)
            msg = jnp.einsum('eb,ebo->eo', comp[edge_type], xb[src])
            key = dst * R + edge_type
            cnt = jax.ops.segment_sum(jnp.ones((msg.shape[0],), x.dtype), key, num_segments=x.shape[0] * R)
            norm = 1.0 / jnp.maximum(cnt, 1.0)
            agg = jax.ops.segment_sum(msg * norm[key][:, None], dst, num_segments=x.shape[0])
            return agg + x @ root + bias
        key = jax.random.key(seed)
        ks = jax.random.split(key, 12)
        s = 0.05
        return {'x': jax.random.normal(ks[0], (N, DIN), jnp.float32), 'edge_index': jax.random.randint(ks[1], (2, E), 0, N, jnp.int64), 'edge_type': jax.random.randint(ks[2], (E,), 0, R, jnp.int64), 'basis1': jax.random.normal(ks[3], (B, DIN, DH), jnp.float32) * s, 'comp1': jax.random.normal(ks[4], (R, B), jnp.float32) * s, 'root1': jax.random.normal(ks[5], (DIN, DH), jnp.float32) * s, 'bias1': jnp.zeros((DH,), jnp.float32), 'basis2': jax.random.normal(ks[6], (B, DH, DOUT), jnp.float32) * s, 'comp2': jax.random.normal(ks[7], (R, B), jnp.float32) * s, 'root2': jax.random.normal(ks[8], (DH, DOUT), jnp.float32) * s, 'bias2': jnp.zeros((DOUT,), jnp.float32)}
    _L3_gnn_all = _L3_gnn_setup()
    _L3_gnn_in = {k: v for k, v in _L3_gnn_all.items() if k in ('basis1', 'comp1', 'root1', 'bias1', 'basis2', 'comp2', 'root2', 'bias2')}
    del _L3_gnn_all
    return {'x': x, 'src': src, 'dst': dst, 'edge_attr_64': edge_attr_64, 'edge_type_8': edge_type_8, 'edge_weight1': edge_weight1, 'L0_gnn_W_in2f': _L0_gnn_in['W_in2f'], 'L0_gnn_Wf1': _L0_gnn_in['Wf1'], 'L0_gnn_bf1': _L0_gnn_in['bf1'], 'L0_gnn_Wf2': _L0_gnn_in['Wf2'], 'L0_gnn_bf2': _L0_gnn_in['bf2'], 'L0_gnn_Wo1': _L0_gnn_in['Wo1'], 'L0_gnn_bo1': _L0_gnn_in['bo1'], 'L0_gnn_Wo2': _L0_gnn_in['Wo2'], 'L0_gnn_bo2': _L0_gnn_in['bo2'], 'L1_gnn_Wq': _L1_gnn_in['Wq'], 'L1_gnn_Wk': _L1_gnn_in['Wk'], 'L1_gnn_Wv': _L1_gnn_in['Wv'], 'L1_gnn_Wp': _L1_gnn_in['Wp'], 'L1_gnn_bp': _L1_gnn_in['bp'], 'L1_gnn_ln1_g': _L1_gnn_in['ln1_g'], 'L1_gnn_ln1_b': _L1_gnn_in['ln1_b'], 'L1_gnn_ln2_g': _L1_gnn_in['ln2_g'], 'L1_gnn_ln2_b': _L1_gnn_in['ln2_b'], 'L1_gnn_W1': _L1_gnn_in['W1'], 'L1_gnn_b1': _L1_gnn_in['b1'], 'L1_gnn_W2': _L1_gnn_in['W2'], 'L1_gnn_b2': _L1_gnn_in['b2'], 'L2_gnn_W_in': _L2_gnn_in['W_in'], 'L2_gnn_b_in': _L2_gnn_in['b_in'], 'L2_gnn_W_agg': _L2_gnn_in['W_agg'], 'L2_gnn_W_self': _L2_gnn_in['W_self'], 'L2_gnn_b_hid': _L2_gnn_in['b_hid'], 'L2_gnn_W_out': _L2_gnn_in['W_out'], 'L2_gnn_b_out': _L2_gnn_in['b_out'], 'L3_gnn_basis1': _L3_gnn_in['basis1'], 'L3_gnn_comp1': _L3_gnn_in['comp1'], 'L3_gnn_root1': _L3_gnn_in['root1'], 'L3_gnn_bias1': _L3_gnn_in['bias1'], 'L3_gnn_basis2': _L3_gnn_in['basis2'], 'L3_gnn_comp2': _L3_gnn_in['comp2'], 'L3_gnn_root2': _L3_gnn_in['root2'], 'L3_gnn_bias2': _L3_gnn_in['bias2']}

def reference(x, src, dst, edge_attr_64, edge_type_8, edge_weight1, L0_gnn_W_in2f, L0_gnn_Wf1, L0_gnn_bf1, L0_gnn_Wf2, L0_gnn_bf2, L0_gnn_Wo1, L0_gnn_bo1, L0_gnn_Wo2, L0_gnn_bo2, L1_gnn_Wq, L1_gnn_Wk, L1_gnn_Wv, L1_gnn_Wp, L1_gnn_bp, L1_gnn_ln1_g, L1_gnn_ln1_b, L1_gnn_ln2_g, L1_gnn_ln2_b, L1_gnn_W1, L1_gnn_b1, L1_gnn_W2, L1_gnn_b2, L2_gnn_W_in, L2_gnn_b_in, L2_gnn_W_agg, L2_gnn_W_self, L2_gnn_b_hid, L2_gnn_W_out, L2_gnn_b_out, L3_gnn_basis1, L3_gnn_comp1, L3_gnn_root1, L3_gnn_bias1, L3_gnn_basis2, L3_gnn_comp2, L3_gnn_root2, L3_gnn_bias2):
    import jax
    import jax.numpy as jnp

    def _L0_gnn_ref(x, rbf, dist_cut, idx_i, idx_j, W_in2f, Wf1, bf1, Wf2, bf2, Wo1, bo1, Wo2, bo2):
        import jax, jax.numpy as jnp
        import numpy as np
        LOG2 = float(np.log(2.0))

        def ssp(x):
            return jax.nn.softplus(x) - LOG2
        N_ATOMS, N_EDGES, N_HF, N_RBF = (25000, 25000, 256, 64)
        n_atoms = x.shape[0]
        h = x @ W_in2f
        Wij = ssp(rbf @ Wf1 + bf1) @ Wf2 + bf2
        Wij = Wij * dist_cut
        x_ij = h[idx_j] * Wij
        m = jax.ops.segment_sum(x_ij, idx_i, num_segments=n_atoms)
        m = ssp(m @ Wo1 + bo1) @ Wo2 + bo2
        return x + m

    def _L1_gnn_ref(h, edge_bias, src, dst, Wq, Wk, Wv, Wp, bp, ln1_g, ln1_b, ln2_g, ln2_b, W1, b1, W2, b2):
        import jax, jax.numpy as jnp
        import numpy as np
        DIM = 256
        H = 8
        HD = DIM // H
        N = 3125
        E = 50000
        FFN = 4 * DIM
        EPS = 1e-05

        def layer_norm(x, g, b):
            mu = jnp.mean(x, axis=-1, keepdims=True)
            var = jnp.mean((x - mu) ** 2, axis=-1, keepdims=True)
            return (x - mu) * jax.lax.rsqrt(var + EPS) * g + b

        def _mhsa(h, edge_bias, src, dst, Wq, Wk, Wv, Wp, bp):
            n = h.shape[0]
            Q = (h @ Wq).reshape(n, H, HD)
            K = (h @ Wk).reshape(n, H, HD)
            V = (h @ Wv).reshape(n, H, HD)
            score = jnp.einsum('ehd,ehd->eh', K[src], Q[dst]) / np.sqrt(HD) + edge_bias
            m = jax.ops.segment_max(score, dst, num_segments=n)
            ex = jnp.exp(score - m[dst])
            denom = jax.ops.segment_sum(ex, dst, num_segments=n)
            attn = ex / denom[dst]
            out = jax.ops.segment_sum(attn[:, :, None] * V[src], dst, num_segments=n)
            return out.reshape(n, DIM) @ Wp + bp
        attn_out = _mhsa(h, edge_bias, src, dst, Wq, Wk, Wv, Wp, bp)
        h1 = layer_norm(h + attn_out, ln1_g, ln1_b)
        ffn_out = jax.nn.gelu(h1 @ W1 + b1, approximate=False) @ W2 + b2
        return layer_norm(h1 + ffn_out, ln2_g, ln2_b)

    def _L2_gnn_ref(x, W_in, b_in, W_agg, W_self, b_hid, W_out, b_out, edge_index):
        import jax, jax.numpy as jnp
        import numpy as np
        N_NODES = 3125
        N_EDGES = 50000
        IN_CH = 256
        HID_CH = 256
        OUT_CH = 256
        N_LAYERS = 3
        n = x.shape[0]
        dst = edge_index[0]
        src = edge_index[1]
        n_layers = W_agg.shape[0]
        h = x @ W_in + b_in
        deg = jax.ops.segment_sum(jnp.ones_like(dst, dtype=h.dtype), dst, num_segments=n)
        deg = jnp.maximum(deg, 1.0)[:, None]
        for l in range(n_layers):
            agg = jax.ops.segment_sum(h[src], dst, num_segments=n) / deg
            h = jax.nn.relu(agg @ W_agg[l] + h @ W_self[l] + b_hid[l])
        return h @ W_out + b_out

    def _L3_gnn_ref(x, edge_index, edge_type, basis1, comp1, root1, bias1, basis2, comp2, root2, bias2):
        import jax, jax.numpy as jnp
        import numpy as np
        N = 3125
        E = 50000
        DIN = 256
        DH = 256
        DOUT = 256
        R = 8
        B = 4

        def rgcn_conv(x, src, dst, edge_type, basis, comp, root, bias):
            xb = jnp.einsum('ni,bio->nbo', x, basis)
            msg = jnp.einsum('eb,ebo->eo', comp[edge_type], xb[src])
            key = dst * R + edge_type
            cnt = jax.ops.segment_sum(jnp.ones((msg.shape[0],), x.dtype), key, num_segments=x.shape[0] * R)
            norm = 1.0 / jnp.maximum(cnt, 1.0)
            agg = jax.ops.segment_sum(msg * norm[key][:, None], dst, num_segments=x.shape[0])
            return agg + x @ root + bias
        src, dst = (edge_index[0], edge_index[1])
        h = rgcn_conv(x, src, dst, edge_type, basis1, comp1, root1, bias1)
        h = jax.nn.relu(h)
        out = rgcn_conv(h, src, dst, edge_type, basis2, comp2, root2, bias2)
        return out
    edge_index = jnp.stack([src, dst])
    x = _layernorm(x + _L0_gnn_ref(x, edge_attr_64, edge_weight1, src, dst, L0_gnn_W_in2f, L0_gnn_Wf1, L0_gnn_bf1, L0_gnn_Wf2, L0_gnn_bf2, L0_gnn_Wo1, L0_gnn_bo1, L0_gnn_Wo2, L0_gnn_bo2), axis=-1)
    x = _layernorm(x + _L1_gnn_ref(x, edge_weight1, src, dst, L1_gnn_Wq, L1_gnn_Wk, L1_gnn_Wv, L1_gnn_Wp, L1_gnn_bp, L1_gnn_ln1_g, L1_gnn_ln1_b, L1_gnn_ln2_g, L1_gnn_ln2_b, L1_gnn_W1, L1_gnn_b1, L1_gnn_W2, L1_gnn_b2), axis=-1)
    x = _layernorm(x + _L2_gnn_ref(x, L2_gnn_W_in, L2_gnn_b_in, L2_gnn_W_agg, L2_gnn_W_self, L2_gnn_b_hid, L2_gnn_W_out, L2_gnn_b_out, edge_index), axis=-1)
    x = _layernorm(x + _L3_gnn_ref(x, edge_index, edge_type_8, L3_gnn_basis1, L3_gnn_comp1, L3_gnn_root1, L3_gnn_bias1, L3_gnn_basis2, L3_gnn_comp2, L3_gnn_root2, L3_gnn_bias2), axis=-1)
    return x

_drawn_inputs = setup_inputs


def setup_inputs(seed=0):
    import zlib

    import numpy as np

    out = dict(_drawn_inputs(seed))
    spreads = {'L0_gnn_bf1': (0.0, 0.27),
     'L0_gnn_bf2': (0.0, 0.1),
     'L0_gnn_bo1': (0.0, 0.267),
     'L0_gnn_bo2': (0.0, 0.1),
     'L1_gnn_bp': (0.0, 0.1),
     'L1_gnn_ln1_g': (1.0, 0.2),
     'L1_gnn_ln1_b': (0.0, 0.1),
     'L1_gnn_ln2_g': (1.0, 0.2),
     'L1_gnn_ln2_b': (0.0, 0.1),
     'L1_gnn_b1': (0.0, 0.287),
     'L1_gnn_b2': (0.0, 0.1),
     'L2_gnn_b_in': (0.0, 0.1),
     'L2_gnn_b_hid': (0.0, 0.1),
     'L2_gnn_b_out': (0.0, 0.1),
     'L3_gnn_bias1': (0.0, 0.1),
     'L3_gnn_bias2': (0.0, 0.1)}
    factors = {}
    for name, (base, spread) in spreads.items():
        noise = np.random.default_rng([zlib.crc32(name.encode()), seed]).standard_normal(out[name].shape)
        drawn = base * np.exp(spread * noise) if base else spread * noise
        out[name] = jnp.asarray(drawn.astype(out[name].dtype))
    for name, factor in factors.items():
        out[name] = (out[name] * factor).astype(out[name].dtype)
    return out
```

```python
import numpy as np
import concourse.bass as bass
from concourse import mybir
from concourse.alu_op_type import AluOpType as ALU
from contextlib import ExitStack, contextmanager

F32 = mybir.dt.float32
I32 = mybir.dt.int32
BF16 = mybir.dt.bfloat16
ACT = mybir.ActivationFunctionType
X = mybir.AxisListType.X

P = 128
D = 256
KT = D // P
H = 8
HD = D // H
R = 8
NBASIS = 4
RBF = 64
FFN = 4 * D
U = 4
EPS = 1e-5
LOG2 = float(np.log(2.0))
BIG = 1e30

D_SRC, D_DST, D_REL, D_LOC, D_W, D_TYPE, D_WORDS = 0, 1, 2, 3, 4, 5, 8
S_IDX, S_LOC, S_W, S_WORDS = RBF, RBF + 1, RBF + 2, RBF + 4


class Core:

    def __init__(self, nc):
        self.nc = nc
        self.phases = 0

    @contextmanager
    def phase(self):
        nc, self.phases = self.nc, self.phases + 1
        tag, taken = f"p{self.phases}_", []
        with ExitStack() as stack:
            class Scope:
                @staticmethod
                def sb(name, shape, dt=F32):
                    return stack.enter_context(nc.sbuf_tensor(tag + name, shape, dt))

                @staticmethod
                def ps(name, shape, dt=F32):
                    return stack.enter_context(nc.psum_tensor(tag + name, shape, dt))

                @staticmethod
                def sem(name):
                    taken.append(nc.alloc_semaphore(name=tag + name))
                    return taken[-1]

                @staticmethod
                def block():
                    return nc.Block()

            yield Scope
            nc.clear_and_free_semaphores(taken)
            nc.all_engine_barrier()


def chain(engine, sem):
    count = [0]

    def link(instruction, signal=None, value=0):
        if signal is None:
            count[0] += 1
            signal, value = sem, count[0]
        instruction.then_inc(signal, 1)
        engine.wait_ge(signal, value)
    return link


def rounds_of(engine, rounds, body):
    body(0)
    with engine.Fori(1, rounds) as i:
        body(i)


def after(engine, sem, value):
    if not isinstance(value, int) or value > 0:
        engine.wait_ge(sem, value)


def bc(ap, axis, n):
    shape = list(ap.shape)
    shape.insert(axis, n)
    return ap.unsqueeze(axis).broadcast_to(shape)


def constants_and_sort(core, g):
    nc = core.nc
    EP, EC, NB, NT = g.EP, g.EC, g.NB, g.NT
    with core.phase() as s:
        tri = s.sb("tri", [EP, P])
        ones = s.sb("ones", [EP, P])
        iota_i = s.sb("iota_i", [P, NT], I32)
        iota_t = s.sb("iota_t", [P, NT])
        begun = s.sb("begun", [P, NT])
        key_i = {k: s.sb(f"key_{k}", [EP, EC], I32) for k in "DS"}
        type_i = s.sb("type_i", [EP, EC], I32)
        weight = s.sb("weight", [EP, EC])
        tmp_i = s.sb("tmp_i", [P, max(EC, NT)], I32)
        blk_f = s.sb("blk_f", [EP, EC])
        loc_f = s.sb("loc_f", [EP, EC])
        pos_f = s.sb("pos_f", [EP, EC])
        low_f = s.sb("low_f", [EP, EC])
        mask = s.sb("mask", [EP, NB * EC], BF16)
        rank = s.sb("rank", [P, NB * max(EC, NT)])
        count = s.sb("count", [EP, NB])
        before = s.sb("before", [EP, NB])
        tiles_i = s.sb("tiles_i", [P, NB], I32)
        tiles_f = s.sb("tiles_f", [P, NB])
        first_t = s.sb("first_t", [P, NB])
        shift = s.sb("shift", [EP, NB])
        blank_d = s.sb("blank_d", [P, g.FILL_D * D_WORDS])
        blank_s = s.sb("blank_s", [P, g.FILL_S * S_WORDS])
        sums = s.ps("sums", [P, 2, NB])
        keys_in, pool_done, dve_step = s.sem("keys_in"), s.sem("pool_done"), s.sem("dve_step")
        counted, summed, blanked, filled = s.sem("counted"), s.sem("summed"), s.sem("blanked"), s.sem("filled")

        def edges(ap):
            return ap.rearrange("(p j) -> p j", p=EP)

        with s.block() as block:
            @block.sync
            def _(sp):
                sp.dma_start(key_i["D"][:, :], edges(g.inp["dst"])).then_inc(keys_in, 16)
                sp.dma_start(key_i["S"][:, :], edges(g.inp["src"])).then_inc(keys_in, 16)
                sp.dma_start(type_i[:, :], edges(g.inp["edge_type_8"])).then_inc(keys_in, 16)
                sp.dma_start(weight[:, :], edges(g.inp["edge_weight1"].rearrange("e o -> (e o)")))\
                    .then_inc(keys_in, 16)
                sp.wait_ge(blanked, 1)
                with sp.Fori(0, NT // g.FILL_D) as i:
                    sp.dma_start(g.rec_d[:, bass.ds(i * (g.FILL_D * D_WORDS), g.FILL_D * D_WORDS)],
                                 blank_d[:, :].bitcast(I32)).then_inc(filled, 16)
                with sp.Fori(0, NT // g.FILL_S) as i:
                    sp.dma_start(g.rec_s[:, bass.ds(i * (g.FILL_S * S_WORDS), g.FILL_S * S_WORDS)],
                                 blank_s[:, :]).then_inc(filled, 16)
                sp.wait_ge(filled, 16 * (NT // g.FILL_D + NT // g.FILL_S))

            @block.gpsimd
            def _(pool):
                link = chain(pool, pool_done)
                link(pool.iota(iota_i[:, :], pattern=[[1, NT]], base=0, channel_multiplier=0))
                link(pool.memset(g.ident[:, :], 0.0))
                link(pool.affine_select(out=g.ident[:, :], in_=g.ident[:, :], compare_op=ALU.not_equal, fill=1.0,
                                        base=0, pattern=[[-1, P]], channel_multiplier=1))
                link(pool.memset(ones[:, :], 1.0))
                link(pool.affine_select(out=tri[:, :], in_=ones[:, :], compare_op=ALU.is_gt, fill=0.0,
                                        base=0, pattern=[[1, P]], channel_multiplier=-1))

            @block.tensor
            def _(pe):
                pe.wait_ge(pool_done, 5)
                for n in range(2):
                    pe.wait_ge(counted, n + 1)
                    pe.matmul(sums[:, 0, :], tri[:, :], count[:, :], start=True, stop=True)
                    pe.matmul(sums[:, 1, :], ones[:, :], count[:, :], start=True, stop=True).then_inc(summed, 1)

            @block.vector
            def _(dve):
                link = chain(dve, dve_step)
                link(dve.memset(blank_s[:, :], 0.0))
                link(dve.memset(blank_d[:, :], 0.0))
                link(dve.memset(blank_d[:, :].rearrange("p (t w) -> p t w", w=D_WORDS)[:, :, D_LOC], -1.0))
                link(dve.memset(blank_d[:, :].rearrange("p (t w) -> p t w", w=D_WORDS)[:, :, D_W], -BIG))
                link(dve.memset(blank_s[:, :].rearrange("p (t w) -> p t w", w=S_WORDS)[:, :, S_LOC], -1.0), blanked, 1)
                dve.wait_ge(pool_done, 2)
                link(dve.tensor_copy(iota_t[:, :], iota_i[:, :]))
                link(dve.tensor_copy(g.iota[:, :], iota_t[:, 0:P]))
                link(dve.memset(g.ones_row[:, :], 1.0))
                dve.wait_ge(pool_done, 3)
                for k in range(U):
                    link(dve.tensor_copy(g.ident4[:, k * P:(k + 1) * P], g.ident[:, :]))
                dve.wait_ge(keys_in, 64)
                link(dve.tensor_copy(g.whole_d[:, :, D_SRC], key_i["S"][:, :]))
                link(dve.tensor_copy(g.whole_d[:, :, D_DST], key_i["D"][:, :]))
                link(dve.scalar_tensor_tensor(out=g.whole_d[:, :, D_REL], in0=key_i["S"][:, :], scalar=float(R),
                                              in1=type_i[:, :], op0=ALU.mult, op1=ALU.add))
                link(dve.tensor_copy(g.float_d[:, :, D_W - D_LOC], weight[:, :]))
                link(dve.tensor_copy(g.float_d[:, :, D_TYPE - D_LOC], type_i[:, :]))
                link(dve.tensor_copy(g.float_s[:, :, 1], weight[:, :]))
                link(dve.tensor_copy(g.whole_s[:, :], key_i["D"][:, :]))
                for n, k in enumerate("DS"):
                    loc_out = g.float_d[:, :, 0] if k == "D" else g.float_s[:, :, 0]
                    blk_out = g.blk_d if k == "D" else g.blk_s
                    ti, mk = tmp_i[0:EP, 0:EC], mask[:, :]
                    rk = rank[0:EP, 0:NB * EC]
                    rk3 = rk.rearrange("p (b j) -> p b j", b=NB)
                    mk3 = mk.rearrange("p (b j) -> p b j", b=NB)
                    link(dve.tensor_scalar(ti, key_i[k][:, :], P - 1, None, ALU.bitwise_and))
                    link(dve.tensor_copy(loc_out, ti))
                    link(dve.tensor_scalar(ti, key_i[k][:, :], 7, None, ALU.arith_shift_right))
                    link(dve.tensor_copy(blk_f[:, :], ti))
                    link(dve.tensor_tensor(mk3, bc(blk_f[:, :], 1, NB), bc(iota_t[0:EP, 0:NB], 2, EC), ALU.is_equal))
                    link(dve.tensor_tensor_scan(rk, mk, mk, 0.0, ALU.add, ALU.max))
                    ends = rk3[:, :, EC - 1]
                    link(dve.tensor_copy(count[:, :], ends))
                    link(dve.tensor_tensor(count[:, 1:NB], ends[:, 1:NB], ends[:, 0:NB - 1], ALU.subtract), counted, n + 1)
                    dve.wait_ge(summed, n + 1)
                    link(dve.tensor_scalar(tiles_i[:, :], sums[:, 1, :], float(P - 1), None, ALU.add))
                    link(dve.tensor_scalar(tiles_i[:, :], tiles_i[:, :], 7, None, ALU.arith_shift_right))
                    link(dve.tensor_copy(tiles_f[:, :], tiles_i[:, :]))
                    link(dve.tensor_tensor_scan(first_t[:, :], tiles_f[:, :], tiles_f[:, :], 0.0, ALU.add, ALU.max))
                    link(dve.tensor_tensor(first_t[:, :], first_t[:, :], tiles_f[:, :], ALU.subtract))
                    link(dve.tensor_tensor(before[:, :], ends, count[:, :], ALU.subtract))
                    link(dve.tensor_tensor(before[:, :], sums[0:EP, 0, :], before[:, :], ALU.subtract))
                    link(dve.scalar_tensor_tensor(out=shift[:, :], in0=first_t[0:EP, :], scalar=float(P),
                                                  in1=before[:, :], op0=ALU.mult, op1=ALU.add))
                    link(dve.tensor_scalar(shift[:, :], shift[:, :], -1.0, None, ALU.add))
                    link(dve.tensor_tensor(rk3, rk3, bc(shift[:, :], 2, EC), ALU.add))
                    link(dve.tensor_tensor(rk, rk, mk, ALU.mult))
                    link(dve.tensor_reduce(pos_f[:, :], rk.rearrange("p (b j) -> p j b", b=NB), X, ALU.add))
                    link(dve.tensor_copy(ti, pos_f[:, :]))
                    link(dve.tensor_scalar(ti, ti, P - 1, None, ALU.bitwise_and))
                    link(dve.tensor_copy(low_f[:, :], ti))
                    link(dve.tensor_copy(ti, pos_f[:, :]))
                    link(dve.tensor_scalar(ti, ti, 7, None, ALU.arith_shift_right))
                    link(dve.scalar_tensor_tensor(out=g.row[:, :, n], in0=low_f[:, :], scalar=float(NT),
                                                  in1=ti, op0=ALU.mult, op1=ALU.add))
                    ge = rank[:, 0:NB * NT]
                    link(dve.tensor_tensor(ge.rearrange("p (b t) -> p b t", b=NB), bc(iota_t[:, :], 1, NB),
                                           bc(first_t[:, :], 2, NT), ALU.is_ge))
                    link(dve.tensor_reduce(begun[:, :], ge.rearrange("p (b t) -> p t b", b=NB), X, ALU.add))
                    link(dve.tensor_scalar(blk_out[:, :], begun[:, :], -1.0, None, ALU.add))


def scatter_records(core, g):
    nc = core.nc
    EP, EC = g.EP, g.EC
    C, RING = g.SC, g.SRING
    rounds = EC // (C * RING)
    with core.phase() as s:
        rd = [s.sb(f"rd{r}", [EP, C, D_WORDS], I32) for r in range(RING)]
        rs = [s.sb(f"rs{r}", [EP, C, S_WORDS]) for r in range(RING)]
        at = [s.sb(f"at{r}", [EP, C, 2], I32) for r in range(RING)]
        attr_in = [s.sem(f"attr_in{r}") for r in range(RING)]
        sent = [s.sem(f"sent{r}") for r in range(RING)]
        built, cleared, back, sending = s.sem("built"), s.sem("cleared"), s.sem("back"), s.sem("sending")
        attr = g.inp["edge_attr_64"].rearrange("(p j) f -> p j f", p=EP)
        per_round = 2 * C * 16

        with s.block() as block:
            @block.sync
            def _(sp):
                def body(i):
                    for r in range(RING):
                        after(sp, sent[r], i * per_round)
                        sp.dma_start(rs[r][:, :, 0:RBF], attr[:, bass.ds(i * (C * RING) + r * C, C), :])\
                            .then_inc(attr_in[r], 16)
                rounds_of(sp, rounds, body)
                for r in range(RING):
                    sp.wait_ge(sent[r], rounds * per_round)
                sp.dma_start(g.edge_d[:, :, :].rearrange("p t w -> p (t w)"), g.rec_d).then_inc(back, 16)
                sp.wait_ge(back, 16)

            @block.vector
            def _(dve):
                for r in range(RING):
                    dve.memset(rd[r][:, :, :], 0).then_inc(cleared, 1)
                    dve.memset(rs[r][:, :, S_W + 1:S_WORDS], 0.0).then_inc(cleared, 1)
                dve.wait_ge(cleared, 2 * RING)
                def body(i):
                    for r in range(RING):
                        c = bass.ds(i * (C * RING) + r * C, C)
                        after(dve, sent[r], i * per_round)
                        dve.tensor_copy(at[r][:, :, :], g.row[:, c, :])
                        dve.tensor_copy(rd[r][:, :, 0:D_LOC], g.whole_d[:, c, :])
                        dve.tensor_copy(rd[r][:, :, D_LOC:D_TYPE + 1].bitcast(F32), g.float_d[:, c, :])
                        dve.tensor_copy(rs[r][:, :, S_IDX:S_IDX + 1].bitcast(I32), g.whole_s[:, c].unsqueeze(2))
                        dve.tensor_copy(rs[r][:, :, S_LOC:S_W + 1], g.float_s[:, c, :]).then_inc(built, 1)
                rounds_of(dve, rounds, body)

            @block.gpsimd
            def _(pool):
                def body(i):
                    for r in range(RING):
                        pool.wait_ge(built, i * RING + r + 1)
                        pool.wait_ge(attr_in[r], i * 16 + 16)
                        pool.sem_inc(sending, 1)
                        for c in range(C):
                            pool.indirect_dma_start(
                                g.rec_d_rows, bass.IndirectOffsetOnAxis(ap=at[r][:, c, 0:1], axis=0),
                                rd[r][:, c, :], None).then_inc(sent[r], 16)
                            pool.indirect_dma_start(
                                g.rec_s_rows, bass.IndirectOffsetOnAxis(ap=at[r][:, c, 1:2], axis=0),
                                rs[r][:, c, :], None).then_inc(sent[r], 16)
                rounds_of(pool, rounds, body)


def load_nodes(core, g):
    whole = g.N // P
    with core.phase() as s:
        zeroed, loaded = s.sem("zeroed"), s.sem("loaded")
        with s.block() as block:
            @block.vector
            def _(dve):
                dve.memset(g.x[:, whole:, :], 0.0).then_inc(zeroed, 1)

            @block.sync
            def _(sp):
                x = g.inp["x"]
                sp.dma_start(g.x[:, 0:whole, :], x[0:whole * P, :].rearrange("(b p) f -> p b f", p=P)).then_inc(loaded, 16)
                sp.wait_ge(zeroed, 1)
                if g.N > whole * P:
                    sp.dma_start(g.x[0:g.N - whole * P, whole, :], x[whole * P:g.N, :]).then_inc(loaded, 16)
                sp.wait_ge(loaded, 16 * (1 + (g.N > whole * P)))


def store_nodes(core, g, src):
    whole = g.N // P
    with core.phase() as s:
        stored = s.sem("stored")
        with s.block() as block:
            @block.sync
            def _(sp):
                sp.dma_start(g.out[0:whole * P, :].rearrange("(b p) f -> p b f", p=P), src[:, 0:whole, :]).then_inc(stored, 16)
                if g.N > whole * P:
                    sp.dma_start(g.out[whole * P:g.N, :], src[0:g.N - whole * P, whole, :]).then_inc(stored, 16)
                sp.wait_ge(stored, 16 * (1 + (g.N > whole * P)))


def linear(core, g, ins, weights, bias=None, func=ACT.Identity, dst=None, tables=(), plus=None, held=None):
    nc, NB, LB = core.nc, g.NB, g.LB
    kts = [a.shape[2] // P for a in ins]
    kt = sum(kts)
    n_out = held.shape[2] if held is not None else sum(w.shape[1] for w in weights[0])
    chunks = [(c, min(c + 512, n_out)) for c in range(0, n_out, 512)]
    per_fill = min(kt, 4)
    fills, oc = kt // per_fill, len(chunks)
    F, G = LB * fills, LB * oc
    RT, RO = 3, 4
    rounds = NB // LB

    def last_use(n, ring, total):
        return max(m for m in range(total) if m % ring == n % ring)

    with core.phase() as s:
        w = held if held is not None else s.sb("w", [P, kt, n_out])
        b_row = s.sb("b_row", [1, n_out]) if bias is not None else None
        stage = [s.sb(f"stage{u}", [P, kt * P]) for u in range(LB)]
        xT = [s.sb(f"xT{u}", [P, kt, P]) for u in range(LB)]
        held_out = [s.sb(f"o{u}", [P, n_out]) for u in range(LB)] if dst is None else None
        psT = [s.ps(f"psT{r}", [P, 512]) for r in range(RT)]
        psO = [s.ps(f"psO{r}", [P, 512]) for r in range(RO)]
        w_in, staged, turned, kept, made, out_done = (
            s.sem(n) for n in ("w_in", "staged", "turned", "kept", "made", "out_done"))
        stored = [s.sem(f"stored{u}") for u in range(LB)]
        n_loads = sum(len(p) for p in weights) if held is None else 0
        n_loads += 0 if bias is None else len(bias)

        def target(i, u, c):
            if dst is None:
                return held_out[u][:, c[0]:c[1]]
            return dst[:, bass.ds(i * LB + u, 1), c[0]:c[1]].rearrange("p o n -> p (o n)")

        with s.block() as block:
            @block.sync
            def _(sp):
                k0 = 0
                if held is None:
                    for k, pieces in zip(kts, weights):
                        c0 = 0
                        for piece in pieces:
                            sp.dma_start(w[:, k0:k0 + k, c0:c0 + piece.shape[1]],
                                         piece.rearrange("(k p) n -> p k n", p=P)).then_inc(w_in, 16)
                            c0 += piece.shape[1]
                        k0 += k
                if bias is not None:
                    c0 = 0
                    for piece in bias:
                        sp.dma_start(b_row[:, c0:c0 + piece.shape[0]], piece.unsqueeze(0)).then_inc(w_in, 16)
                        c0 += piece.shape[0]
                if n_loads:
                    sp.wait_ge(w_in, 16 * n_loads)
                if tables:
                    def body(i):
                        for u in range(LB):
                            sp.wait_ge(out_done, i * G + G + (u + 1) * oc)
                            c0 = 0
                            for t in tables:
                                n = t.shape[1]
                                sp.dma_start(t[bass.ds((i * LB + u) * P, P), :], target(i, u, (c0, c0 + n)))\
                                    .then_inc(stored[u], 16)
                                c0 += n
                    rounds_of(sp, rounds, body)
                    for u in range(LB):
                        sp.wait_ge(stored[u], 16 * len(tables) * rounds)

            def evacuate(eng, i, on_act):
                for u in range(LB):
                    for c, ch in enumerate(chunks):
                        n = u * oc + c
                        eng.wait_ge(made, i * G + G + n + 1)
                        if tables:
                            after(eng, stored[u], i * (16 * len(tables)))
                        src = psO[n % RO][:, 0:ch[1] - ch[0]]
                        if on_act:
                            eng.activation(target(i, u, ch), src, func).then_inc(out_done, 1)
                        else:
                            more = plus[:, bass.ds(i * LB + u, 1), ch[0]:ch[1]].rearrange("p o n -> p (o n)")
                            eng.tensor_tensor(target(i, u, ch), src, more, ALU.add).then_inc(out_done, 1)

            @block.scalar
            def _(act):
                if plus is None:
                    act.sem_inc(out_done, G)
                def body(i):
                    for u in range(LB):
                        act.wait_ge(turned, i * F + (u + 1) * fills)
                        k0 = 0
                        for a, k in zip(ins, kts):
                            step = act.activation(stage[u][:, k0 * P:(k0 + k) * P],
                                                  a[:, bass.ds(i * LB + u, 1), :].rearrange("p o n -> p (o n)"),
                                                  ACT.Copy)
                            k0 += k
                        step.then_inc(staged, 1)
                    if plus is None:
                        evacuate(act, i, True)
                rounds_of(act, rounds, body)

            @block.tensor
            def _(pe):
                pe.sem_inc(turned, F)
                pe.sem_inc(made, G)
                if n_loads:
                    pe.wait_ge(w_in, 16 * n_loads)
                def body(i):
                    for u in range(LB):
                        pe.wait_ge(staged, i * LB + u + 1)
                        for f in range(fills):
                            n = u * fills + f
                            if n < RT:
                                pe.wait_ge(kept, i * F + last_use(n, RT, F) + 1)
                            else:
                                pe.wait_ge(kept, i * F + F + n - RT + 1)
                            for k in range(per_fill):
                                c = (f * per_fill + k) * P
                                step = pe.transpose(psT[n % RT][:, k * P:(k + 1) * P], stage[u][:, c:c + P], g.ident[:, :])
                            step.then_inc(turned, 1)
                    for u in range(LB):
                        pe.wait_ge(kept, i * F + F + (u + 1) * fills)
                        for c, (c0, c1) in enumerate(chunks):
                            n = u * oc + c
                            if n < RO:
                                pe.wait_ge(out_done, i * G + last_use(n, RO, G) + 1)
                            else:
                                pe.wait_ge(out_done, i * G + G + n - RO + 1)
                            o = psO[n % RO][:, 0:c1 - c0]
                            if bias is not None:
                                pe.matmul(o, g.ones_row[:, :], b_row[:, c0:c1], start=True, stop=False)
                            for k in range(kt):
                                step = pe.matmul(o, xT[u][:, k, :], w[:, k, c0:c1], start=(bias is None and k == 0),
                                                 stop=(k == kt - 1))
                            step.then_inc(made, 1)
                rounds_of(pe, rounds, body)

            @block.vector
            def _(dve):
                dve.sem_inc(kept, F)
                if plus is not None:
                    dve.sem_inc(out_done, G)
                def body(i):
                    for u in range(LB):
                        for f in range(fills):
                            n = u * fills + f
                            dve.wait_ge(turned, i * F + F + n + 1)
                            dve.wait_ge(made, i * G + (u + 1) * oc)
                            dve.tensor_copy(xT[u][:, f * per_fill:(f + 1) * per_fill, :].rearrange("p k n -> p (k n)"),
                                            psT[n % RT][:, 0:per_fill * P]).then_inc(kept, 1)
                    if plus is not None:
                        evacuate(dve, i, False)
                rounds_of(dve, rounds, body)


def layer_norm(s, link, act_turn, dve, x, spare, mean, rstd, gain=None, shift=None):
    flat = "p b f -> p (b f)"
    NB = x.shape[1]
    link(dve.tensor_reduce(mean, x, X, ALU.add))
    link(dve.tensor_scalar(mean, mean, 1.0 / D, None, ALU.mult))
    link(dve.tensor_tensor(x, x, bc(mean, 2, D), ALU.subtract))
    link(dve.tensor_tensor(spare, x, x, ALU.mult))
    link(dve.tensor_reduce(rstd, spare, X, ALU.add))
    act_turn(dve.tensor_scalar(rstd, rstd, 1.0 / D, EPS, ALU.mult, ALU.add))
    link(dve.reciprocal(rstd, rstd))
    link(dve.tensor_tensor(x, x, bc(rstd, 2, D), ALU.mult))
    if gain is not None:
        link(dve.tensor_tensor(x, x, bc(gain, 1, NB), ALU.mult))
        link(dve.tensor_tensor(x, x, bc(shift, 1, NB), ALU.add))


def norms(core, g, steps):
    with core.phase() as s:
        mean, rstd = s.sb("mean", [P, g.NB]), s.sb("rstd", [P, g.NB])
        rows = {}
        for n, (_, _, _, _, gain, shift) in enumerate(steps):
            if gain is not None:
                rows[n] = (s.sb(f"gain{n}", [P, D]), s.sb(f"shift{n}", [P, D]))
        rows_in, dve_step, asked, rooted = s.sem("rows_in"), s.sem("dve_step"), s.sem("asked"), s.sem("rooted")
        with s.block() as block:
            @block.sync
            def _(sp):
                for n, (a, b) in rows.items():
                    sp.dma_start(a[:, :], steps[n][4].partition_broadcast(P)).then_inc(rows_in, 16)
                    sp.dma_start(b[:, :], steps[n][5].partition_broadcast(P)).then_inc(rows_in, 16)
                if rows:
                    sp.wait_ge(rows_in, 32 * len(rows))

            @block.scalar
            def _(act):
                for n in range(len(steps)):
                    act.wait_ge(asked, n + 1)
                    act.activation(rstd[:, :], rstd[:, :], ACT.Sqrt).then_inc(rooted, 1)

            @block.vector
            def _(dve):
                link = chain(dve, dve_step)
                turns = [0]

                def act_turn(instruction):
                    turns[0] += 1
                    instruction.then_inc(asked, 1)
                    dve.wait_ge(rooted, turns[0])

                if rows:
                    dve.wait_ge(rows_in, 32 * len(rows))
                for n, (x, spare, y, c, _, _) in enumerate(steps):
                    if y is not None:
                        link(dve.scalar_tensor_tensor(out=x[:, :, :], in0=x[:, :, :], scalar=float(c), in1=y[:, :, :],
                                                      op0=ALU.mult, op1=ALU.add))
                    gain, shift = rows.get(n, (None, None))
                    layer_norm(s, link, act_turn, dve, x[:, :, :], spare[:, :, :], mean[:, :], rstd[:, :],
                               None if gain is None else gain[:, :], None if gain is None else shift[:, :])


def softplus_less_log2(core, g, x, spare):
    with core.phase() as s:
        act_step, topped, done = s.sem("act_step"), s.sem("topped"), s.sem("done")
        with s.block() as block:
            @block.scalar
            def _(act):
                link = chain(act, act_step)
                link(act.activation(spare[:, :, :], x[:, :, :], ACT.Abs))
                link(act.activation(spare[:, :, :], spare[:, :, :], ACT.Exp, scale=-1.0))
                link(act.activation(spare[:, :, :], spare[:, :, :], ACT.Ln, bias=1.0))

            @block.vector
            def _(dve):
                dve.wait_ge(act_step, 1)
                dve.tensor_scalar(x[:, :, :], x[:, :, :], 0.0, -LOG2, ALU.max, ALU.add).then_inc(topped, 1)
                dve.wait_ge(topped, 1)
                dve.wait_ge(act_step, 3)
                dve.tensor_tensor(x[:, :, :], x[:, :, :], spare[:, :, :], ALU.add).then_inc(done, 1)
                dve.wait_ge(done, 1)


def filter_pass(core, g, acc, table):
    nc, NT = core.nc, g.NT
    rounds = NT // (2 * U)
    Q = range(2)
    with core.phase() as s:
        wf1 = s.sb("wf1", [RBF, D])
        bf1 = s.sb("bf1", [P, KT])
        wf2 = s.sb("wf2", [P, KT, D])
        bf2 = s.sb("bf2", [1, D])
        rest = s.sb("rest", [1, 2, D])
        parts = s.sb("parts", [1, 3, D], BF16)
        bf2_3 = s.sb("bf2_3", [3, D], BF16)
        ones_3 = s.sb("ones_3", [3, P], BF16)
        half = s.sb("half", [P, 1])
        rec = [s.sb(f"rec{q}", [P, U, S_WORDS]) for q in Q]
        hg = [s.sb(f"hg{q}", [P, U, D]) for q in Q]
        rT = [s.sb(f"rT{q}", [RBF, U * P]) for q in Q]
        soft = [s.sb(f"soft{q}", [P, KT, U * P]) for q in Q]
        top = [s.sb(f"top{q}", [P, KT, U * P]) for q in Q]
        hid = [s.sb(f"hid{q}", [P, KT, U * P]) for q in Q]
        msg = [s.sb(f"msg{q}", [P, U, D + 1]) for q in Q]
        hot = [s.sb(f"hot{q}", [P, U, P]) for q in Q]
        psR = s.ps("psR", [RBF, U * P])
        psH = s.ps("psH", [P, KT, U * P])
        psW = s.ps("psW", [P, U, D])
        psA = [s.ps(f"psA{r}", [P, 512]) for r in range(2)]
        w_in, dve_step, split, moved, cleared = (s.sem(n) for n in ("w_in", "dve_step", "split", "moved", "cleared"))
        turn = [s.sem(f"turn_{e}") for e in ("pool", "pe", "sp")]
        loaded, gathered, turned, copied, hidden, absed, exped, lned, topped, hidded, filtered, saved, hotted, msged = (
            [s.sem(f"{n}{q}") for q in Q] for n in (
                "loaded", "gathered", "turned", "copied", "hidden", "absed", "exped", "lned", "topped", "hidded",
                "filtered", "saved", "hotted", "msged"))
        summed = [s.sem(f"summed{r}") for r in range(2)]
        added = [s.sem(f"added{r}") for r in range(2)]

        def before(sems, i, q):
            return (sems[1], i) if q == 0 else (sems[0], i + 1)

        with s.block() as block:
            @block.sync
            def _(sp):
                sp.dma_start(wf1[:, :], g.inp["L0_gnn_Wf1"]).then_inc(w_in, 16)
                sp.dma_start(bf1[:, :], g.inp["L0_gnn_bf1"].rearrange("(k p) -> p k", p=P),
                             allow_slow_non_contiguous=True).then_inc(w_in, 16)
                sp.dma_start(wf2[:, :, :], g.inp["L0_gnn_Wf2"].rearrange("(k p) n -> p k n", p=P)).then_inc(w_in, 16)
                sp.dma_start(bf2[:, :], g.inp["L0_gnn_bf2"].unsqueeze(0)).then_inc(w_in, 16)
                sp.wait_ge(split, 1)
                for k in range(3):
                    sp.dma_start(bf2_3[k:k + 1, :], parts[0:1, k, :]).then_inc(moved, 16)
                sp.wait_ge(moved, 48)
                def body(i):
                    for q in Q:
                        after(sp, gathered[q], i * (16 * U))
                        after(sp, msged[q], i)
                        after(sp, turned[q], i)
                        sp.sem_inc(turn[2], 1)
                        sp.dma_start(rec[q][:, :, :].rearrange("p t w -> p (t w)"),
                                     g.rec_s[:, bass.ds(i * (2 * U * S_WORDS) + q * U * S_WORDS, U * S_WORDS)])\
                            .then_inc(loaded[q], 16)
                rounds_of(sp, rounds, body)

            @block.gpsimd
            def _(pool):
                def body(i):
                    for q in Q:
                        pool.wait_ge(loaded[q], i * 16 + 16)
                        after(pool, msged[q], i)
                        pool.sem_inc(turn[0], 1)
                        for u in range(U):
                            pool.indirect_dma_start(
                                hg[q][:, u, :], None, table,
                                bass.IndirectOffsetOnAxis(ap=rec[q][:, u, S_IDX:S_IDX + 1].bitcast(I32), axis=0))\
                                .then_inc(gathered[q], 16)
                rounds_of(pool, rounds, body)

            @block.tensor
            def _(pe):
                pe.wait_ge(w_in, 64)
                pe.wait_ge(moved, 48)
                pe.wait_ge(cleared, 5)
                def body(i):
                    for q in Q:
                        pe.wait_ge(loaded[q], i * 16 + 16)
                        after(pe, *before(copied, i, q))
                        pe.sem_inc(turn[1], 1)
                        for u in range(U):
                            step = pe.transpose(psR[:, u * P:(u + 1) * P], rec[q][:, u, 0:RBF], g.ident[:, :])
                        step.then_inc(turned[q], 1)
                        pe.wait_ge(copied[q], i + 1)
                        after(pe, *before(topped, i, q))
                        for k in range(KT):
                            step = pe.matmul(psH[:, k, :], wf1[:, k * P:(k + 1) * P], rT[q][:, :], start=True, stop=True)
                        step.then_inc(hidden[q], 1)
                    for q in Q:
                        pe.wait_ge(hidded[q], i + 1)
                        after(pe, *before(msged, i, q))
                        for u in range(U):
                            pe.matmul(psW[:, u, :], ones_3[:, :], bf2_3[:, :], start=True, stop=False)
                            for k in range(KT):
                                step = pe.matmul(psW[:, u, :], hid[q][:, k, u * P:(u + 1) * P], wf2[:, k, :],
                                                 start=False, stop=(k == KT - 1))
                        step.then_inc(filtered[q], 1)
                    for q in Q:
                        pe.wait_ge(msged[q], i + 1)
                        pe.wait_ge(hotted[q], i + 1)
                        for u in range(U):
                            after(pe, added[u % 2], i * (2 * U // 2) + q * U // 2 + u // 2)
                            pe.matmul(psA[u % 2][:, 0:D + 1], hot[q][:, u, :], msg[q][:, u, :], start=True, stop=True)\
                                .then_inc(summed[u % 2], 1)
                rounds_of(pe, rounds, body)

            @block.scalar
            def _(act):
                act.wait_ge(cleared, 5)

                def copy_radial(i, q):
                    act.wait_ge(turned[q], i + 1)
                    after(act, hidden[q], i)
                    act.activation(rT[q][:, :], psR[:, :], ACT.Copy).then_inc(copied[q], 1)

                def take_abs(i, q):
                    act.wait_ge(topped[q], i + 1)
                    after(act, hidded[q], i)
                    act.activation(soft[q][:, :, :], top[q][:, :, :], ACT.Abs).then_inc(absed[q], 1)

                def take_soft(i, q):
                    act.wait_ge(absed[q], i + 1)
                    act.activation(soft[q][:, :, :], soft[q][:, :, :], ACT.Exp, scale=-1.0).then_inc(exped[q], 1)
                    act.wait_ge(exped[q], i + 1)
                    act.activation(soft[q][:, :, :], soft[q][:, :, :], ACT.Ln, scale=0.5, bias=half[:, 0:1]).then_inc(lned[q], 1)

                def body(i):
                    copy_radial(i, 0)
                    take_abs(i, 0)
                    copy_radial(i, 1)
                    take_soft(i, 0)
                    take_abs(i, 1)
                    take_soft(i, 1)
                rounds_of(act, rounds, body)

            @block.vector
            def _(dve):
                link = chain(dve, dve_step)
                dve.memset(half[:, :], 0.5).then_inc(cleared, 1)
                dve.memset(ones_3[:, :], 1.0).then_inc(cleared, 1)
                dve.memset(acc[:, :, :], 0.0).then_inc(cleared, 1)
                for q in Q:
                    dve.memset(msg[q][:, :, D:D + 1], 1.0).then_inc(cleared, 1)
                dve.wait_ge(w_in, 64)
                link(dve.tensor_copy(parts[:, 0, :], bf2[:, :]))
                link(dve.tensor_tensor(rest[:, 0, :], bf2[:, :], parts[:, 0, :], ALU.subtract))
                link(dve.tensor_copy(parts[:, 1, :], rest[:, 0, :]))
                link(dve.tensor_tensor(rest[:, 1, :], rest[:, 0, :], parts[:, 1, :], ALU.subtract))
                link(dve.tensor_copy(parts[:, 2, :], rest[:, 1, :]), split, 1)
                dve.wait_ge(cleared, 5)

                def first(i, q):
                    dve.wait_ge(loaded[q], i * 16 + 16)
                    t = bass.ds(i * (2 * U) + q * U, U)
                    dve.tensor_copy(g.idx_s[:, t], rec[q][:, :, S_IDX].bitcast(I32)).then_inc(saved[q], 1)
                    dve.tensor_copy(g.loc_s[:, t], rec[q][:, :, S_LOC]).then_inc(saved[q], 1)
                    for u in range(U):
                        step = dve.tensor_scalar(hot[q][:, u, :], g.iota[:, :], rec[q][:, u, S_LOC:S_LOC + 1], None,
                                                 ALU.is_equal)
                    step.then_inc(hotted[q], 1)
                    dve.wait_ge(hidden[q], i + 1)
                    for k in range(KT):
                        step = dve.tensor_scalar(top[q][:, k, :], psH[:, k, :], bf1[:, k:k + 1], None, ALU.add)
                    step.then_inc(topped[q], 1)

                def hide(i, q):
                    dve.wait_ge(topped[q], i + 1)
                    dve.wait_ge(lned[q], i + 1)
                    after(dve, filtered[q], i)
                    dve.scalar_tensor_tensor(out=hid[q][:, :, :], in0=top[q][:, :, :], scalar=0.0, in1=soft[q][:, :, :],
                                             op0=ALU.max, op1=ALU.add).then_inc(hidded[q], 1)

                def messages(i, q):
                    dve.wait_ge(filtered[q], i + 1)
                    dve.wait_ge(gathered[q], i * (16 * U) + 16 * U)
                    for u in range(U):
                        step = dve.scalar_tensor_tensor(out=msg[q][:, u, 0:D], in0=psW[:, u, :],
                                                        scalar=rec[q][:, u, S_W:S_W + 1], in1=hg[q][:, u, :],
                                                        op0=ALU.mult, op1=ALU.mult)
                    step.then_inc(msged[q], 1)

                def add(i, q):
                    for u in range(U):
                        done = i * U + q * (U // 2) + u // 2
                        b = dve.value_load(g.blk_s[0:1, bass.ds(i * (2 * U) + q * U + u, 1)], min_val=0, max_val=g.NB - 1)
                        dve.wait_ge(summed[u % 2], done + 1)
                        after(dve, added[(u + 1) % 2], done + (1 if u % 2 else 0))
                        a = acc[:, bass.ds(b, 1), 0:D + 1].rearrange("p o n -> p (o n)")
                        dve.tensor_tensor(a, a, psA[u % 2][:, 0:D + 1], ALU.add).then_inc(added[u % 2], 1)

                def body(i):
                    first(i, 0)
                    hide(i, 0)
                    first(i, 1)
                    hide(i, 1)
                    messages(i, 0)
                    messages(i, 1)
                    add(i, 0)
                    add(i, 1)
                rounds_of(dve, rounds, body)



def aggregate_pass(core, g, acc, table, idx, loc, blk, weight=None):
    nc, NT = core.nc, g.NT
    rounds = NT // (2 * U)
    Q = range(2)
    with core.phase() as s:
        at = [s.sb(f"at{q}", [P, U], I32) for q in Q]
        rows = [s.sb(f"rows{q}", [P, U, D]) for q in Q]
        hot = [s.sb(f"hot{q}", [P, U, P]) for q in Q]
        psA = [s.ps(f"psA{u}", [P, 512]) for u in range(U)]
        staged, gathered, hotted = ([s.sem(f"{n}{q}") for q in Q] for n in ("staged", "gathered", "hotted"))
        summed = [s.sem(f"summed{u}") for u in range(U)]
        added = [s.sem(f"added{u}") for u in range(U)]
        cleared, turn = s.sem("cleared"), s.sem("turn")
        with s.block() as block:
            @block.scalar
            def _(act):
                def body(i):
                    for q in Q:
                        after(act, gathered[q], i * (16 * U))
                        act.activation(at[q][:, :], idx[:, bass.ds(i * (2 * U) + q * U, U)], ACT.Copy)\
                            .then_inc(staged[q], 1)
                rounds_of(act, rounds, body)

            @block.gpsimd
            def _(pool):
                def body(i):
                    for q in Q:
                        pool.wait_ge(staged[q], i + 1)
                        pool.wait_ge(summed[U - 1], i * 2 + q + 1)
                        pool.sem_inc(turn, 1)
                        for u in range(U):
                            pool.indirect_dma_start(rows[q][:, u, :], None, table,
                                                    bass.IndirectOffsetOnAxis(ap=at[q][:, u:u + 1], axis=0))\
                                .then_inc(gathered[q], 16)
                rounds_of(pool, rounds, body)

            @block.tensor
            def _(pe):
                for u in range(U):
                    pe.sem_inc(summed[u], 2)
                def body(i):
                    for q in Q:
                        pe.wait_ge(hotted[q], i + 1)
                        pe.wait_ge(gathered[q], i * (16 * U) + 16 * U)
                        for u in range(U):
                            after(pe, added[u], i * 2 + q)
                            pe.matmul(psA[u][:, 0:D], hot[q][:, u, :], rows[q][:, u, :], start=True, stop=True)\
                                .then_inc(summed[u], 1)
                rounds_of(pe, rounds, body)

            @block.vector
            def _(dve):
                dve.memset(acc[:, :, 0:D], 0.0).then_inc(cleared, 1)
                dve.wait_ge(cleared, 1)
                def body(i):
                    for q in Q:
                        dve.wait_ge(summed[U - 1], i * 2 + q + 1)
                        for u in range(U):
                            t = bass.ds(i * (2 * U) + q * U + u, 1)
                            if weight is None:
                                step = dve.tensor_scalar(hot[q][:, u, :], g.iota[:, :], loc[:, t], None, ALU.is_equal)
                            else:
                                step = dve.tensor_scalar(hot[q][:, u, :], g.iota[:, :], loc[:, t], weight[:, t],
                                                         ALU.is_equal, ALU.mult)
                        step.then_inc(hotted[q], 1)
                    for q in Q:
                        for u in range(U):
                            b = dve.value_load(blk[0:1, bass.ds(i * (2 * U) + q * U + u, 1)], min_val=0, max_val=g.NB - 1)
                            dve.wait_ge(summed[u], i * 2 + q + 3)
                            after(dve, added[(u - 1) % U], i * 2 + q + (1 if u else 0))
                            a = acc[:, bass.ds(b, 1), 0:D].rearrange("p o n -> p (o n)")
                            dve.tensor_tensor(a, a, psA[u][:, 0:D], ALU.add).then_inc(added[u], 1)
                rounds_of(dve, rounds, body)


def score_pass(core, g, q_table, k_table, score, top, type_hot):
    nc, NT = core.nc, g.NT
    rounds = NT // (2 * U)
    Q = range(2)
    edge_f = g.edge_d[:, :, :].bitcast(F32)
    with core.phase() as s:
        at = [s.sb(f"at{q}", [P, U, 2], I32) for q in Q]
        kg = [s.sb(f"kg{q}", [P, U, D]) for q in Q]
        qg = [s.sb(f"qg{q}", [P, U, D]) for q in Q]
        part = [s.sb(f"part{q}", [P, U, H]) for q in Q]
        sc = [s.sb(f"sc{q}", [P, U, H]) for q in Q]
        cold = [s.sb(f"cold{q}", [P, U, P], BF16) for q in Q]
        hot = [s.sb(f"hot{q}", [P, U, P], BF16) for q in Q]
        best = s.sb("best", [P, 2, H])
        psM = [s.ps(f"psM{r}", [P, H, P]) for r in range(2)]
        psC = [s.ps(f"psC{r}", [P, 512]) for r in range(2)]
        staged, gathered, multiplied, reduced, scored, kept, masked = (
            [s.sem(f"{n}{q}") for q in Q] for n in (
                "staged", "gathered", "multiplied", "reduced", "scored", "kept", "masked"))
        spread, found, maxed, counted = ([s.sem(f"{n}{r}") for r in range(2)] for n in ("spread", "found", "maxed", "counted"))
        cleared, turn = s.sem("cleared"), s.sem("turn")
        with s.block() as block:
            @block.scalar
            def _(act):
                def body(i):
                    for q in Q:
                        after(act, gathered[q], i * (2 * 16 * U))
                        act.activation(at[q][:, :, :], g.edge_d[:, bass.ds(i * (2 * U) + q * U, U), D_SRC:D_DST + 1],
                                       ACT.Copy).then_inc(staged[q], 1)
                    for q in Q:
                        act.wait_ge(scored[q], i + 1)
                        act.activation(score[:, bass.ds(i * (2 * U) + q * U, U), :], sc[q][:, :, :], ACT.Copy)\
                            .then_inc(kept[q], 1)
                rounds_of(act, rounds, body)

            @block.gpsimd
            def _(pool):
                def body(i):
                    for q in Q:
                        pool.wait_ge(staged[q], i + 1)
                        after(pool, multiplied[q], i)
                        pool.sem_inc(turn, 1)
                        for u in range(U):
                            for n, (rows, table) in enumerate(((kg, k_table), (qg, q_table))):
                                pool.indirect_dma_start(rows[q][:, u, :], None, table,
                                                        bass.IndirectOffsetOnAxis(ap=at[q][:, u, n:n + 1], axis=0))\
                                    .then_inc(gathered[q], 16)
                rounds_of(pool, rounds, body)

            @block.tensor
            def _(pe):
                pe.wait_ge(cleared, 2)
                def body(i):
                    for q in Q:
                        pe.wait_ge(masked[q], i + 1)
                        pe.wait_ge(scored[q], i + 1)
                        for u in range(U):
                            r, done = u % 2, i * U + q * (U // 2) + u // 2
                            after(pe, found[r], done)
                            for h in range(0, H, 4):
                                pe.matmul(psM[r][:, h:h + 4, :].rearrange("p h e -> p (h e)"), cold[q][:, u, :],
                                          g.ident4[:, :], start=True, stop=False)
                            for h in range(H):
                                step = pe.matmul(psM[r][:, h, :], sc[q][:, u, h:h + 1].broadcast_to([P, P]), g.ident[:, :],
                                                 start=False, stop=(h % 4 == 3))
                            step.then_inc(spread[r], 1)
                            after(pe, counted[r], done)
                            pe.matmul(psC[r][:, 0:R], hot[q][:, u, :],
                                      type_hot[:, bass.ds(i * (2 * U) + q * U + u, 1), :].rearrange("p o n -> p (o n)"),
                                      start=True, stop=True).then_inc(maxed[r], 1)
                rounds_of(pe, rounds, body)

            @block.vector
            def _(dve):
                types = edge_f[:, :, D_TYPE]
                dve.tensor_tensor(type_hot[:, :, :], bc(types, 2, R), bc(g.iota[:, 0:R], 1, NT), ALU.is_equal)\
                    .then_inc(cleared, 1)
                dve.memset(top[:, :, 0:H], -BIG)
                dve.memset(top[:, :, H:H + R], 0.0).then_inc(cleared, 1)
                dve.wait_ge(cleared, 2)

                def scores(i, q):
                    t = bass.ds(i * (2 * U) + q * U, U)
                    for u in range(U):
                        tu = bass.ds(i * (2 * U) + q * U + u, 1)
                        dve.tensor_scalar(cold[q][:, u, :], g.iota[:, :], edge_f[:, tu, D_LOC], -BIG,
                                          ALU.not_equal, ALU.mult)
                        step = dve.tensor_scalar(hot[q][:, u, :], g.iota[:, :], edge_f[:, tu, D_LOC], None, ALU.is_equal)
                    step.then_inc(masked[q], 1)
                    dve.wait_ge(gathered[q], i * (2 * 16 * U) + 2 * 16 * U)
                    dve.tensor_tensor(kg[q][:, :, :], kg[q][:, :, :], qg[q][:, :, :], ALU.mult).then_inc(reduced[q], 1)
                    dve.wait_ge(reduced[q], i + 1)
                    dve.tensor_reduce(part[q][:, :, :], kg[q][:, :, :].rearrange("p u (h d) -> p u h d", h=H), X, ALU.add)\
                        .then_inc(multiplied[q], 1)
                    dve.wait_ge(multiplied[q], i + 1)
                    after(dve, kept[q], i)
                    dve.scalar_tensor_tensor(out=sc[q][:, :, :], in0=part[q][:, :, :], scalar=float(HD) ** -0.5,
                                             in1=bc(edge_f[:, t, D_W], 2, H), op0=ALU.mult, op1=ALU.add)\
                        .then_inc(scored[q], 1)

                def tops(i, q):
                    for u in range(U):
                        r, done = u % 2, i * U + q * (U // 2) + u // 2
                        b = dve.value_load(g.blk_d[0:1, bass.ds(i * (2 * U) + q * U + u, 1)], min_val=0, max_val=g.NB - 1)
                        dve.wait_ge(spread[r], done + 1)
                        dve.tensor_reduce(best[:, r, :], psM[r][:, :, :], X, ALU.max).then_inc(found[r], 1)
                        dve.wait_ge(found[r], done + 1)
                        after(dve, counted[(u + 1) % 2], done + (1 if u % 2 else 0))
                        a = top[:, bass.ds(b, 1), 0:H].rearrange("p o n -> p (o n)")
                        c = top[:, bass.ds(b, 1), H:H + R].rearrange("p o n -> p (o n)")
                        dve.tensor_tensor(a, a, best[:, r, :], ALU.max)
                        dve.wait_ge(maxed[r], done + 1)
                        dve.tensor_tensor(c, c, psC[r][:, 0:R], ALU.add).then_inc(counted[r], 1)

                def body(i):
                    scores(i, 0)
                    scores(i, 1)
                    tops(i, 0)
                    tops(i, 1)
                rounds_of(dve, rounds, body)


def value_pass(core, g, acc, v_table, score, top, type_hot):
    nc, NT = core.nc, g.NT
    rounds = NT // (2 * U)
    Q = range(2)
    edge_f = g.edge_d[:, :, :].bitcast(F32)
    with core.phase() as s:
        at = [s.sb(f"at{q}", [P, U], I32) for q in Q]
        vg = [s.sb(f"vg{q}", [P, U, D]) for q in Q]
        val = [s.sb(f"val{q}", [P, U, D + H]) for q in Q]
        hot = [s.sb(f"hot{q}", [P, U, P]) for q in Q]
        hotT = [s.sb(f"hotT{q}", [P, U, P]) for q in Q]
        less = [s.sb(f"less{q}", [P, U, H]) for q in Q]
        mine = [s.sb(f"mine{q}", [P, U, R]) for q in Q]
        psT = [s.ps(f"psT{q}", [P, U, P]) for q in Q]
        psE = [s.ps(f"psE{q}", [P, 512]) for q in Q]
        psA = [s.ps(f"psA{u}", [P, 512]) for u in range(U)]
        staged, gathered, hotted, turned, copied, spread, lowered, expd, weighed, normed = (
            [s.sem(f"{n}{q}") for q in Q] for n in (
                "staged", "gathered", "hotted", "turned", "copied", "spread", "lowered", "expd", "weighed", "normed"))
        summed = [s.sem(f"summed{u}") for u in range(U)]
        added = [s.sem(f"added{u}") for u in range(U)]
        cleared, turn, dve_step = s.sem("cleared"), s.sem("turn"), s.sem("dve_step")
        with s.block() as block:
            @block.scalar
            def _(act):
                def body(i):
                    for q in Q:
                        after(act, gathered[q], i * (16 * U))
                        act.activation(at[q][:, :], g.edge_d[:, bass.ds(i * (2 * U) + q * U, U), D_SRC], ACT.Copy)\
                            .then_inc(staged[q], 1)
                    for q in Q:
                        act.wait_ge(turned[q], i + 1)
                        after(act, spread[q], i)
                        act.activation(hotT[q][:, :, :], psT[q][:, :, :], ACT.Copy).then_inc(copied[q], 1)
                    for q in Q:
                        act.wait_ge(lowered[q], i + 1)
                        act.wait_ge(summed[U - 1], i * 2 + q + 1)
                        act.activation(val[q][:, :, D:D + H], less[q][:, :, :], ACT.Exp).then_inc(expd[q], 1)
                rounds_of(act, rounds, body)

            @block.gpsimd
            def _(pool):
                def body(i):
                    for q in Q:
                        pool.wait_ge(staged[q], i + 1)
                        after(pool, weighed[q], i)
                        pool.sem_inc(turn, 1)
                        for u in range(U):
                            pool.indirect_dma_start(vg[q][:, u, :], None, v_table,
                                                    bass.IndirectOffsetOnAxis(ap=at[q][:, u:u + 1], axis=0))\
                                .then_inc(gathered[q], 16)
                rounds_of(pool, rounds, body)

            @block.tensor
            def _(pe):
                for u in range(U):
                    pe.sem_inc(summed[u], 2)
                pe.wait_ge(cleared, 1)
                def body(i):
                    for q in Q:
                        pe.wait_ge(hotted[q], i + 1)
                        after(pe, copied[q], i)
                        for u in range(U):
                            step = pe.transpose(psT[q][:, u, :], hot[q][:, u, :], g.ident[:, :])
                        step.then_inc(turned[q], 1)
                    for q in Q:
                        pe.wait_ge(copied[q], i + 1)
                        after(pe, normed[q], i)
                        after(pe, lowered[q], i)
                        for u in range(U):
                            b = pe.value_load(g.blk_d[0:1, bass.ds(i * (2 * U) + q * U + u, 1)], min_val=0, max_val=g.NB - 1)
                            step = pe.matmul(psE[q][:, u * (H + R):(u + 1) * (H + R)], hotT[q][:, u, :],
                                             top[:, bass.ds(b, 1), :].rearrange("p o n -> p (o n)"), start=True, stop=True)
                        step.then_inc(spread[q], 1)
                    for q in Q:
                        pe.wait_ge(weighed[q], i + 1)
                        for u in range(U):
                            after(pe, added[u], i * 2 + q)
                            pe.matmul(psA[u][:, 0:D + H], hot[q][:, u, :], val[q][:, u, :], start=True, stop=True)\
                                .then_inc(summed[u], 1)
                rounds_of(pe, rounds, body)

            @block.vector
            def _(dve):
                inv = top[:, :, H:H + R]
                link = chain(dve, dve_step)
                link(dve.tensor_scalar(inv, inv, 1.0, None, ALU.max))
                link(dve.reciprocal(inv, inv))
                link(dve.memset(acc[:, :, :], 0.0), cleared, 1)

                def hots(i, q):
                    dve.wait_ge(summed[U - 1], i * 2 + q + 1)
                    for u in range(U):
                        tu = bass.ds(i * (2 * U) + q * U + u, 1)
                        step = dve.tensor_scalar(hot[q][:, u, :], g.iota[:, :], edge_f[:, tu, D_LOC], None, ALU.is_equal)
                    step.then_inc(hotted[q], 1)

                def lower(i, q):
                    t = bass.ds(i * (2 * U) + q * U, U)
                    e = psE[q][:, 0:U * (H + R)].rearrange("p (u n) -> p u n", u=U)
                    dve.wait_ge(spread[q], i + 1)
                    after(dve, expd[q], i)
                    dve.tensor_tensor(less[q][:, :, :], score[:, t, :], e[:, :, 0:H], ALU.subtract).then_inc(lowered[q], 1)
                    dve.tensor_tensor(mine[q][:, :, :], e[:, :, H:H + R], type_hot[:, t, :], ALU.mult).then_inc(normed[q], 1)
                    dve.wait_ge(normed[q], i + 1)
                    dve.tensor_reduce(g.norm[:, t], mine[q][:, :, :], X, ALU.add)

                def weigh(i, q):
                    dve.wait_ge(gathered[q], i * (16 * U) + 16 * U)
                    dve.wait_ge(expd[q], i + 1)
                    dve.tensor_tensor(val[q][:, :, 0:D].rearrange("p u (h d) -> p u h d", h=H),
                                      vg[q][:, :, :].rearrange("p u (h d) -> p u h d", h=H),
                                      bc(val[q][:, :, D:D + H], 3, HD), ALU.mult).then_inc(weighed[q], 1)

                def add(i, q):
                    for u in range(U):
                        b = dve.value_load(g.blk_d[0:1, bass.ds(i * (2 * U) + q * U + u, 1)], min_val=0, max_val=g.NB - 1)
                        dve.wait_ge(summed[u], i * 2 + q + 3)
                        after(dve, added[(u - 1) % U], i * 2 + q + (1 if u else 0))
                        a = acc[:, bass.ds(b, 1), :].rearrange("p o n -> p (o n)")
                        dve.tensor_tensor(a, a, psA[u][:, 0:D + H], ALU.add).then_inc(added[u], 1)

                def body(i):
                    for step in (hots, lower, weigh, add):
                        for q in Q:
                            step(i, q)
                rounds_of(dve, rounds, body)


def divide_heads(core, g, acc):
    with core.phase() as s:
        step = s.sem("step")
        with s.block() as block:
            @block.vector
            def _(dve):
                link = chain(dve, step)
                den, num = acc[:, :, D:D + H], acc[:, :, 0:D].rearrange("p b (h d) -> p b h d", h=H)
                link(dve.tensor_scalar(den, den, 1e-30, None, ALU.max))
                link(dve.reciprocal(den, den))
                link(dve.tensor_tensor(num, num, bc(den, 3, HD), ALU.mult))


def scale_nodes(core, g, acc, factor):
    with core.phase() as s:
        step = s.sem("step")
        with s.block() as block:
            @block.vector
            def _(dve):
                link = chain(dve, step)
                link(dve.tensor_tensor(acc[:, :, 0:D], acc[:, :, 0:D], bc(factor, 2, D), ALU.mult))


def degrees(core, g, acc):
    with core.phase() as s:
        step = s.sem("step")
        with s.block() as block:
            @block.vector
            def _(dve):
                link = chain(dve, step)
                link(dve.tensor_scalar(g.inv_degree[:, :], acc[:, :, D], 1.0, None, ALU.max))
                link(dve.reciprocal(g.inv_degree[:, :], g.inv_degree[:, :]))


def positive_part(core, g, x):
    with core.phase() as s:
        step = s.sem("step")
        with s.block() as block:
            @block.vector
            def _(dve):
                chain(dve, step)(dve.tensor_scalar(x[:, :, :], x[:, :, :], 0.0, None, ALU.max))


def relation_weights(core, g, basis, comp, made):
    with core.phase() as s:
        base = s.sb("base", [P, NBASIS, KT, D])
        c = s.sb("c", [P, R * NBASIS])
        loaded, step = s.sem("loaded"), s.sem("step")
        with s.block() as block:
            @block.sync
            def _(sp):
                for n in range(NBASIS):
                    sp.dma_start(base[:, n, :, :], basis[n].rearrange("(k p) n -> p k n", p=P)).then_inc(loaded, 16)
                sp.dma_start(c[:, :], comp.rearrange("r b -> (r b)").partition_broadcast(P)).then_inc(loaded, 16)
                sp.wait_ge(loaded, 16 * (NBASIS + 1))

            @block.vector
            def _(dve):
                link = chain(dve, step)
                dve.wait_ge(loaded, 16 * (NBASIS + 1))
                for r in range(R):
                    o = made[:, :, r * D:(r + 1) * D]
                    link(dve.tensor_scalar(o, base[:, 0, :, :], c[:, r * NBASIS:r * NBASIS + 1], None, ALU.mult))
                    for n in range(1, NBASIS):
                        link(dve.scalar_tensor_tensor(out=o, in0=base[:, n, :, :],
                                                      scalar=c[:, r * NBASIS + n:r * NBASIS + n + 1], in1=o,
                                                      op0=ALU.mult, op1=ALU.add))


class Graph:
    pass


def graph_layers(nc, inp, out):
    core, g = Core(nc), Graph()
    g.inp, g.out = inp, out
    g.N, g.E = inp["x"].shape[0], inp["src"].shape[0]
    g.NB = -(-g.N // P)
    g.NPAD = g.NB * P
    g.EP = max(p for p in range(1, P + 1) if g.E % p == 0)
    g.EC = g.E // g.EP
    body = 2 * U
    g.NT = -(-((g.E + g.NB * (P - 1)) // P) // body) * body
    g.SC, g.SRING = 5, 5
    g.LB = max(n for n in range(1, 6) if g.NB % n == 0)
    g.FILL_D, g.FILL_S = g.NT // 8, g.NT // 22

    def scratch(name, shape, dt=F32):
        return nc.dram_tensor(name, shape, dt, kind="Internal").ap()

    rec_d = scratch("rec_d", (P * g.NT, D_WORDS), I32)
    rec_s = scratch("rec_s", (P * g.NT, S_WORDS))
    g.rec_d_rows, g.rec_s_rows = rec_d, rec_s
    g.rec_d = rec_d.rearrange("(p t) w -> p (t w)", p=P)
    g.rec_s = rec_s.rearrange("(p t) w -> p (t w)", p=P)

    with ExitStack() as stay:
        def sb(name, shape, dt=F32):
            return stay.enter_context(nc.sbuf_tensor(name, shape, dt))

        g.ident = sb("ident", [P, P])
        g.ident4 = sb("ident4", [P, U * P], BF16)
        g.iota = sb("iota", [P, P])
        g.ones_row = sb("ones_row", [1, P])
        g.blk_d = sb("blk_d", [P, g.NT], I32)
        g.blk_s = sb("blk_s", [P, g.NT], I32)
        g.edge_d = sb("edge_d", [P, g.NT, D_WORDS], I32)
        with ExitStack() as early:
            def esb(name, shape, dt=F32):
                return early.enter_context(nc.sbuf_tensor(name, shape, dt))

            g.whole_d = esb("whole_d", [g.EP, g.EC, 3], I32)
            g.float_d = esb("float_d", [g.EP, g.EC, 3])
            g.whole_s = esb("whole_s", [g.EP, g.EC], I32)
            g.float_s = esb("float_s", [g.EP, g.EC, 2])
            g.row = esb("row", [g.EP, g.EC, 2], I32)
            constants_and_sort(core, g)
            scatter_records(core, g)

        g.idx_s = sb("idx_s", [P, g.NT], I32)
        g.loc_s = sb("loc_s", [P, g.NT])
        g.norm = sb("norm", [P, g.NT])
        g.inv_degree = sb("inv_degree", [P, g.NB])
        g.x = sb("nodes", [P, g.NB, D])
        big = [sb(f"big{n}", [P, g.NB, D]) for n in range(2)]
        w = g.inp
        h_table, q_table, k_table, v_table = (scratch(n, (g.NPAD, D)) for n in ("h_table", "q_table", "k_table", "v_table"))
        tables = [scratch(f"table{n}", (g.NPAD, D)) for n in range(3)]
        rel_tables = [scratch(f"rel_table{n}", (g.NPAD, R * D)) for n in range(2)]
        load_nodes(core, g)

        linear(core, g, [g.x[:, :, :]], [[w["L0_gnn_W_in2f"]]], tables=[h_table])
        with nc.sbuf_tensor("acc0", [P, g.NB, D + 1], F32) as acc:
            filter_pass(core, g, acc, h_table)
            degrees(core, g, acc)
            linear(core, g, [acc[:, :, 0:D]], [[w["L0_gnn_Wo1"]]], [w["L0_gnn_bo1"]], dst=big[0])
        softplus_less_log2(core, g, big[0], big[1])
        linear(core, g, [big[0][:, :, :]], [[w["L0_gnn_Wo2"]]], [w["L0_gnn_bo2"]], dst=big[1])
        norms(core, g, [(g.x, big[0], big[1], 2.0, None, None)])

        linear(core, g, [g.x[:, :, :]], [[w["L1_gnn_Wq"], w["L1_gnn_Wk"], w["L1_gnn_Wv"]]],
               tables=[q_table, k_table, v_table])
        with nc.sbuf_tensor("top", [P, g.NB, H + R], F32) as top, \
                nc.sbuf_tensor("score", [P, g.NT, H], F32) as score, \
                nc.sbuf_tensor("type_hot", [P, g.NT, R], BF16) as type_hot, \
                nc.sbuf_tensor("acc1", [P, g.NB, D + H], F32) as acc:
            score_pass(core, g, q_table, k_table, score, top, type_hot)
            value_pass(core, g, acc, v_table, score, top, type_hot)
            divide_heads(core, g, acc)
            linear(core, g, [acc[:, :, 0:D]], [[w["L1_gnn_Wp"]]], [w["L1_gnn_bp"]], dst=big[0], plus=g.x)
        norms(core, g, [(big[0], big[1], None, 1.0, w["L1_gnn_ln1_g"], w["L1_gnn_ln1_b"])])
        half = FFN // 2
        with nc.sbuf_tensor("ffn", [P, g.NB, half], F32) as ffn:
            linear(core, g, [big[0][:, :, :]], [[w["L1_gnn_W1"][:, 0:half]]], [w["L1_gnn_b1"][0:half]], ACT.Gelu, dst=ffn)
            linear(core, g, [ffn[:, :, :]], [[w["L1_gnn_W2"][0:half, :]]], [w["L1_gnn_b2"]], dst=big[1], plus=big[0])
            linear(core, g, [big[0][:, :, :]], [[w["L1_gnn_W1"][:, half:FFN]]], [w["L1_gnn_b1"][half:FFN]], ACT.Gelu, dst=ffn)
            linear(core, g, [ffn[:, :, :]], [[w["L1_gnn_W2"][half:FFN, :]]], dst=big[1], plus=big[1])
        norms(core, g, [(big[1], big[0], None, 1.0, w["L1_gnn_ln2_g"], w["L1_gnn_ln2_b"]),
                        (g.x, big[0], big[1], 1.0, None, None)])

        with nc.sbuf_tensor("acc2", [P, g.NB, D], F32) as acc:
            h, other = big
            linear(core, g, [g.x[:, :, :]], [[w["L2_gnn_W_in"]]], [w["L2_gnn_b_in"]], dst=h, tables=[tables[0]])
            for n in range(w["L2_gnn_W_agg"].shape[0]):
                aggregate_pass(core, g, acc, tables[n], g.idx_s, g.loc_s, g.blk_s)
                scale_nodes(core, g, acc, g.inv_degree[:, :])
                last = n == w["L2_gnn_W_agg"].shape[0] - 1
                linear(core, g, [acc[:, :, :], h[:, :, :]], [[w["L2_gnn_W_agg"][n]], [w["L2_gnn_W_self"][n]]],
                       [w["L2_gnn_b_hid"][n]], ACT.Relu, dst=other, tables=[] if last else [tables[n + 1]])
                h, other = other, h
            linear(core, g, [h[:, :, :]], [[w["L2_gnn_W_out"]]], [w["L2_gnn_b_out"]], dst=other, plus=g.x)
            norms(core, g, [(other, h, None, 1.0, None, None)])

            x3, h = other, h
            idx, loc = g.edge_d[:, :, D_REL], g.edge_d[:, :, :].bitcast(F32)[:, :, D_LOC]
            for n, src in enumerate((x3, h)):
                with nc.sbuf_tensor(f"rel{n}", [P, KT, R * D], F32) as rel:
                    relation_weights(core, g, w[f"L3_gnn_basis{n + 1}"], w[f"L3_gnn_comp{n + 1}"], rel)
                    linear(core, g, [src[:, :, :]], None, held=rel, tables=[rel_tables[n]])
                aggregate_pass(core, g, acc, rel_tables[n].rearrange("n (r f) -> (n r) f", r=R), idx, loc, g.blk_d,
                               g.norm[:, :])
                to = h if n == 0 else g.x
                linear(core, g, [src[:, :, :]], [[w[f"L3_gnn_root{n + 1}"]]], [w[f"L3_gnn_bias{n + 1}"]], dst=to, plus=acc)
                if n == 0:
                    positive_part(core, g, h)
            norms(core, g, [(g.x, h, x3, 1.0, None, None)])
        store_nodes(core, g, g.x)


def kernel(**inputs):
    import numpy as _np
    import concourse.bacc as _bacc
    from concourse import mybir as _mybir
    from concourse.bass_utils import run_bass_kernel_spmd as _run

    nc = _bacc.Bacc("TRN2", target_bir_lowering=False, num_devices=1)
    arrays, aps = {}, {}
    for name in inputs:
        a = _np.ascontiguousarray(inputs[name])
        arrays[name] = a
        aps[name] = nc.dram_tensor(name, a.shape, _mybir.dt.from_np(a.dtype), kind="ExternalInput").ap()
    out = nc.dram_tensor("out", inputs["x"].shape, _mybir.dt.float32, kind="ExternalOutput").ap()
    graph_layers(nc, aps, out)
    r = _run(nc, [arrays], core_ids=[0])
    return r.results[0]["out"]
```
